# Optimizing a Trainium2 kernel written in Bass

```python
import numpy as np
import jax
import jax.numpy as jnp

def _softmax(x, axis=-1):
    return jax.nn.softmax(x, axis=axis)

def _gelu(x):
    return jax.nn.gelu(x, approximate=True)

def _silu(x):
    return jax.nn.silu(x)

def _sigmoid(x):
    return jax.nn.sigmoid(x)

def _layernorm(x, axis=-1, eps=1e-05):
    m = jnp.mean(x, axis=axis, keepdims=True)
    v = jnp.var(x, axis=axis, keepdims=True)
    return (x - m) / jnp.sqrt(v + eps)

def _scatter_add(tgt, idx, src, axis=0):
    return tgt.at[idx].add(src)

def _segment_sum(src, seg, n):
    return jax.ops.segment_sum(src, seg, n)
kernel_name = 'mk_rec_standalone_d1_rec_r8_857b22'

def setup_inputs(seed: int=0):
    np.random.seed(seed)
    _w = jnp.asarray

    def _rec_inputs():
        import jax
        import jax.numpy as jnp
        _rk = jax.random.key(seed)
        r_x = jnp.stack([jax.random.randint(jax.random.fold_in(jax.random.fold_in(_rk, 1), 0), (1024,), 8, 4992, jnp.int32), jax.random.randint(jax.random.fold_in(jax.random.fold_in(_rk, 1), 1), (1024,), 138, 40001, jnp.int32), jax.random.randint(jax.random.fold_in(jax.random.fold_in(_rk, 1), 2), (1024,), 9, 39986, jnp.int32), jax.random.randint(jax.random.fold_in(jax.random.fold_in(_rk, 1), 3), (1024,), 140, 39909, jnp.int32), jax.random.randint(jax.random.fold_in(jax.random.fold_in(_rk, 1), 4), (1024,), 46, 39997, jnp.int32), jax.random.randint(jax.random.fold_in(jax.random.fold_in(_rk, 1), 5), (1024,), 73, 39997, jnp.int32), jax.random.randint(jax.random.fold_in(jax.random.fold_in(_rk, 1), 6), (1024,), 49, 39958, jnp.int32), jax.random.randint(jax.random.fold_in(jax.random.fold_in(_rk, 1), 7), (1024,), 4, 39877, jnp.int32), jax.random.randint(jax.random.fold_in(jax.random.fold_in(_rk, 1), 8), (1024,), 36, 39950, jnp.int32), jax.random.randint(jax.random.fold_in(jax.random.fold_in(_rk, 1), 9), (1024,), 10, 39885, jnp.int32), jax.random.randint(jax.random.fold_in(jax.random.fold_in(_rk, 1), 10), (1024,), 24, 39999, jnp.int32), jax.random.randint(jax.random.fold_in(jax.random.fold_in(_rk, 1), 11), (1024,), 47, 39985, jnp.int32), jax.random.randint(jax.random.fold_in(jax.random.fold_in(_rk, 1), 12), (1024,), 60, 39917, jnp.int32), jax.random.randint(jax.random.fold_in(jax.random.fold_in(_rk, 1), 13), (1024,), 60, 39998, jnp.int32), jax.random.randint(jax.random.fold_in(jax.random.fold_in(_rk, 1), 14), (1024,), 14, 39940, jnp.int32), jax.random.randint(jax.random.fold_in(jax.random.fold_in(_rk, 1), 15), (1024,), 71, 39977, jnp.int32), jax.random.randint(jax.random.fold_in(jax.random.fold_in(_rk, 1), 16), (1024,), 103, 39989, jnp.int32), jax.random.randint(jax.random.fold_in(jax.random.fold_in(_rk, 1), 17), (1024,), 2, 39995, jnp.int32), jax.random.randint(jax.random.fold_in(jax.random.fold_in(_rk, 1), 18), (1024,), 94, 39954, jnp.int32), jax.random.randint(jax.random.fold_in(jax.random.fold_in(_rk, 1), 19), (1024,), 70, 39990, jnp.int32), jax.random.randint(jax.random.fold_in(jax.random.fold_in(_rk, 1), 20), (1024,), 27, 39993, jnp.int32), jax.random.randint(jax.random.fold_in(jax.random.fold_in(_rk, 1), 21), (1024,), 0, 39970, jnp.int32), jax.random.randint(jax.random.fold_in(jax.random.fold_in(_rk, 1), 22), (1024,), 94, 40001, jnp.int32), jax.random.randint(jax.random.fold_in(jax.random.fold_in(_rk, 1), 23), (1024,), 17, 39986, jnp.int32), jax.random.randint(jax.random.fold_in(jax.random.fold_in(_rk, 1), 24), (1024,), 38, 39995, jnp.int32), jax.random.randint(jax.random.fold_in(jax.random.fold_in(_rk, 1), 25), (1024,), 7, 40001, jnp.int32), jax.random.randint(jax.random.fold_in(jax.random.fold_in(_rk, 1), 26), (1024,), 18, 39962, jnp.int32), jax.random.randint(jax.random.fold_in(jax.random.fold_in(_rk, 1), 27), (1024,), 20, 39979, jnp.int32), jax.random.randint(jax.random.fold_in(jax.random.fold_in(_rk, 1), 28), (1024,), 11, 4998, jnp.int32), jax.random.randint(jax.random.fold_in(jax.random.fold_in(_rk, 1), 29), (1024,), 49, 39977, jnp.int32), jax.random.randint(jax.random.fold_in(jax.random.fold_in(_rk, 1), 30), (1024,), 3, 4991, jnp.int32), jax.random.randint(jax.random.fold_in(jax.random.fold_in(_rk, 1), 31), (1024,), 12, 39945, jnp.int32), jax.random.randint(jax.random.fold_in(jax.random.fold_in(_rk, 1), 32), (1024,), 47, 4995, jnp.int32), jax.random.randint(jax.random.fold_in(jax.random.fold_in(_rk, 1), 33), (1024,), 14, 39985, jnp.int32), jax.random.randint(jax.random.fold_in(jax.random.fold_in(_rk, 1), 34), (1024,), 165, 39881, jnp.int32), jax.random.randint(jax.random.fold_in(jax.random.fold_in(_rk, 1), 35), (1024,), 73, 39988, jnp.int32), jax.random.randint(jax.random.fold_in(jax.random.fold_in(_rk, 1), 36), (1024,), 22, 39949, jnp.int32), jax.random.randint(jax.random.fold_in(jax.random.fold_in(_rk, 1), 37), (1024,), 22, 39997, jnp.int32), jax.random.randint(jax.random.fold_in(jax.random.fold_in(_rk, 1), 38), (1024,), 15, 39877, jnp.int32), jax.random.randint(jax.random.fold_in(jax.random.fold_in(_rk, 1), 39), (1024,), 1, 39991, jnp.int32), jax.random.randint(jax.random.fold_in(jax.random.fold_in(_rk, 1), 40), (1024,), 70, 39853, jnp.int32), jax.random.randint(jax.random.fold_in(jax.random.fold_in(_rk, 1), 41), (1024,), 11, 4999, jnp.int32), jax.random.randint(jax.random.fold_in(jax.random.fold_in(_rk, 1), 42), (1024,), 164, 39998, jnp.int32), jax.random.randint(jax.random.fold_in(jax.random.fold_in(_rk, 1), 43), (1024,), 67, 39857, jnp.int32), jax.random.randint(jax.random.fold_in(jax.random.fold_in(_rk, 1), 44), (1024,), 7, 39999, jnp.int32), jax.random.randint(jax.random.fold_in(jax.random.fold_in(_rk, 1), 45), (1024,), 61, 39929, jnp.int32), jax.random.randint(jax.random.fold_in(jax.random.fold_in(_rk, 1), 46), (1024,), 0, 39986, jnp.int32), jax.random.randint(jax.random.fold_in(jax.random.fold_in(_rk, 1), 47), (1024,), 15, 4999, jnp.int32), jax.random.randint(jax.random.fold_in(jax.random.fold_in(_rk, 1), 48), (1024,), 80, 4989, jnp.int32), jax.random.randint(jax.random.fold_in(jax.random.fold_in(_rk, 1), 49), (1024,), 69, 39999, jnp.int32), jax.random.randint(jax.random.fold_in(jax.random.fold_in(_rk, 1), 50), (1024,), 113, 39998, jnp.int32), jax.random.randint(jax.random.fold_in(jax.random.fold_in(_rk, 1), 51), (1024,), 110, 39911, jnp.int32), jax.random.randint(jax.random.fold_in(jax.random.fold_in(_rk, 1), 52), (1024,), 36, 39989, jnp.int32), jax.random.randint(jax.random.fold_in(jax.random.fold_in(_rk, 1), 53), (1024,), 24, 39998, jnp.int32), jax.random.randint(jax.random.fold_in(jax.random.fold_in(_rk, 1), 54), (1024,), 25, 39946, jnp.int32), jax.random.randint(jax.random.fold_in(jax.random.fold_in(_rk, 1), 55), (1024,), 50, 40001, jnp.int32), jax.random.randint(jax.random.fold_in(jax.random.fold_in(_rk, 1), 56), (1024,), 42, 39958, jnp.int32), jax.random.randint(jax.random.fold_in(jax.random.fold_in(_rk, 1), 57), (1024,), 45, 39978, jnp.int32), jax.random.randint(jax.random.fold_in(jax.random.fold_in(_rk, 1), 58), (1024,), 49, 39983, jnp.int32), jax.random.randint(jax.random.fold_in(jax.random.fold_in(_rk, 1), 59), (1024,), 28, 39996, jnp.int32), jax.random.randint(jax.random.fold_in(jax.random.fold_in(_rk, 1), 60), (1024,), 30, 5000, jnp.int32), jax.random.randint(jax.random.fold_in(jax.random.fold_in(_rk, 1), 61), (1024,), 28, 39947, jnp.int32), jax.random.randint(jax.random.fold_in(jax.random.fold_in(_rk, 1), 62), (1024,), 24, 39973, jnp.int32), jax.random.randint(jax.random.fold_in(jax.random.fold_in(_rk, 1), 63), (1024,), 5, 39983, jnp.int32), jax.random.randint(jax.random.fold_in(jax.random.fold_in(_rk, 1), 64), (1024,), 12, 39940, jnp.int32), jax.random.randint(jax.random.fold_in(jax.random.fold_in(_rk, 1), 65), (1024,), 72, 39998, jnp.int32), jax.random.randint(jax.random.fold_in(jax.random.fold_in(_rk, 1), 66), (1024,), 10, 39991, jnp.int32), jax.random.randint(jax.random.fold_in(jax.random.fold_in(_rk, 1), 67), (1024,), 5, 4993, jnp.int32), jax.random.randint(jax.random.fold_in(jax.random.fold_in(_rk, 1), 68), (1024,), 3, 39993, jnp.int32), jax.random.randint(jax.random.fold_in(jax.random.fold_in(_rk, 1), 69), (1024,), 9, 39966, jnp.int32), jax.random.randint(jax.random.fold_in(jax.random.fold_in(_rk, 1), 70), (1024,), 35, 39986, jnp.int32), jax.random.randint(jax.random.fold_in(jax.random.fold_in(_rk, 1), 71), (1024,), 0, 39997, jnp.int32), jax.random.randint(jax.random.fold_in(jax.random.fold_in(_rk, 1), 72), (1024,), 10, 39951, jnp.int32), jax.random.randint(jax.random.fold_in(jax.random.fold_in(_rk, 1), 73), (1024,), 3, 4988, jnp.int32), jax.random.randint(jax.random.fold_in(jax.random.fold_in(_rk, 1), 74), (1024,), 13, 39857, jnp.int32), jax.random.randint(jax.random.fold_in(jax.random.fold_in(_rk, 1), 75), (1024,), 40, 39921, jnp.int32), jax.random.randint(jax.random.fold_in(jax.random.fold_in(_rk, 1), 76), (1024,), 17, 39957, jnp.int32), jax.random.randint(jax.random.fold_in(jax.random.fold_in(_rk, 1), 77), (1024,), 19, 39996, jnp.int32), jax.random.randint(jax.random.fold_in(jax.random.fold_in(_rk, 1), 78), (1024,), 32, 4996, jnp.int32), jax.random.randint(jax.random.fold_in(jax.random.fold_in(_rk, 1), 79), (1024,), 32, 39930, jnp.int32), jax.random.randint(jax.random.fold_in(jax.random.fold_in(_rk, 1), 80), (1024,), 78, 39980, jnp.int32), jax.random.randint(jax.random.fold_in(jax.random.fold_in(_rk, 1), 81), (1024,), 7, 39921, jnp.int32), jax.random.randint(jax.random.fold_in(jax.random.fold_in(_rk, 1), 82), (1024,), 39, 39957, jnp.int32), jax.random.randint(jax.random.fold_in(jax.random.fold_in(_rk, 1), 83), (1024,), 29, 39953, jnp.int32), jax.random.randint(jax.random.fold_in(jax.random.fold_in(_rk, 1), 84), (1024,), 2, 39861, jnp.int32), jax.random.randint(jax.random.fold_in(jax.random.fold_in(_rk, 1), 85), (1024,), 33, 39916, jnp.int32), jax.random.randint(jax.random.fold_in(jax.random.fold_in(_rk, 1), 86), (1024,), 76, 39910, jnp.int32), jax.random.randint(jax.random.fold_in(jax.random.fold_in(_rk, 1), 87), (1024,), 9, 39828, jnp.int32), jax.random.randint(jax.random.fold_in(jax.random.fold_in(_rk, 1), 88), (1024,), 74, 4998, jnp.int32), jax.random.randint(jax.random.fold_in(jax.random.fold_in(_rk, 1), 89), (1024,), 30, 4991, jnp.int32), jax.random.randint(jax.random.fold_in(jax.random.fold_in(_rk, 1), 90), (1024,), 82, 39965, jnp.int32), jax.random.randint(jax.random.fold_in(jax.random.fold_in(_rk, 1), 91), (1024,), 19, 39979, jnp.int32), jax.random.randint(jax.random.fold_in(jax.random.fold_in(_rk, 1), 92), (1024,), 17, 39999, jnp.int32), jax.random.randint(jax.random.fold_in(jax.random.fold_in(_rk, 1), 93), (1024,), 5, 39971, jnp.int32), jax.random.randint(jax.random.fold_in(jax.random.fold_in(_rk, 1), 94), (1024,), 39, 39930, jnp.int32), jax.random.randint(jax.random.fold_in(jax.random.fold_in(_rk, 1), 95), (1024,), 10, 40001, jnp.int32), jax.random.randint(jax.random.fold_in(jax.random.fold_in(_rk, 1), 96), (1024,), 77, 39930, jnp.int32), jax.random.randint(jax.random.fold_in(jax.random.fold_in(_rk, 1), 97), (1024,), 88, 39930, jnp.int32), jax.random.randint(jax.random.fold_in(jax.random.fold_in(_rk, 1), 98), (1024,), 0, 39969, jnp.int32), jax.random.randint(jax.random.fold_in(jax.random.fold_in(_rk, 1), 99), (1024,), 3, 39988, jnp.int32)], axis=1)
        return r_x
    r_x = _rec_inputs()

    def _L0_rec_setup():
        import jax, jax.numpy as jnp
        import numpy as np
        B, M, N, D, C = (1024, 100, 5000, 256, 625)
        key = jax.random.key(seed)
        ks = jax.random.split(key, 5)
        x = jax.random.randint(ks[0], (B, M), 0, N + 1)
        s1 = 1.0 / np.sqrt(N).astype(np.float32)
        W1 = jax.random.uniform(ks[1], (D, N), minval=-s1, maxval=s1, dtype=jnp.float32)
        b1 = jax.random.uniform(ks[2], (D,), minval=-s1, maxval=s1, dtype=jnp.float32)
        s2 = 1.0 / np.sqrt(D).astype(np.float32)
        W2 = jax.random.uniform(ks[3], (C, D), minval=-s2, maxval=s2, dtype=jnp.float32)
        b2 = jax.random.uniform(ks[4], (C,), minval=-s2, maxval=s2, dtype=jnp.float32)
        return {'x': x, 'W1': W1, 'b1': b1, 'W2': W2, 'b2': b2}
    _L0_rec_all = _L0_rec_setup()
    _L0_rec_in = {k: v for k, v in _L0_rec_all.items() if k in ('W1', 'b1', 'W2', 'b2')}
    del _L0_rec_all
    return {'r_x': r_x, 'L0_rec_W1': _L0_rec_in['W1'], 'L0_rec_b1': _L0_rec_in['b1'], 'L0_rec_W2': _L0_rec_in['W2'], 'L0_rec_b2': _L0_rec_in['b2']}

def reference(r_x, L0_rec_W1, L0_rec_b1, L0_rec_W2, L0_rec_b2):
    import jax
    import jax.numpy as jnp

    def _L0_rec_ref(x, W1, b1, W2, b2):
        import jax, jax.numpy as jnp
        import numpy as np
        B, M, N, D, C = (1024, 100, 5000, 256, 625)
        b, n = (x.shape[0], W1.shape[1])
        bipr = jnp.zeros((b, n + 1), jnp.float32)
        bipr = bipr.at[jnp.arange(b)[:, None], x].set(1.0)
        bipr = bipr[:, :-1]
        h = bipr @ W1.T + b1
        return h @ W2.T + b2
    y = _L0_rec_ref(r_x, L0_rec_W1, L0_rec_b1, L0_rec_W2, L0_rec_b2)
    return y

_drawn_inputs = setup_inputs


def setup_inputs(seed=0):
    import zlib

    import numpy as np

    out = dict(_drawn_inputs(seed))
    spreads = {}
    factors = {}
    for name, (base, spread) in spreads.items():
        noise = np.random.default_rng([zlib.crc32(name.encode()), seed]).standard_normal(out[name].shape)
        drawn = base * np.exp(spread * noise) if base else spread * noise
        out[name] = jnp.asarray(drawn.astype(out[name].dtype))
    for name, factor in factors.items():
        out[name] = (out[name] * factor).astype(out[name].dtype)
    return out
```

```python
import concourse.bass as bass
import concourse.mybir as mybir
from contextlib import ExitStack

BATCH, IDS, N_IDS, D, CLASSES = 1024, 100, 5000, 256, 625
P = 128
LO = 128
LO_BITS = 7
HI = -(-N_IDS // LO)
TILE = 128
TILES = BATCH // TILE
BANK = 512
D_HALVES = D // P
CUT = min(CLASSES, BANK)

HOT_ROWS = 32
HOT_SLOTS = 4
HOT_STEPS = TILE // HOT_ROWS
COUNT_ROWS = 16
COUNT_SLOTS = 2
COUNT_STEPS = TILE // COUNT_ROWS
ROWS_PER_BANK = COUNT_ROWS // 2
CHUNKS = 8
CHUNK_HI = HI // CHUNKS
STAGES = 2
HI_CUTS = [0, 4, 8, 13, 18, 23, 28, 34, 40]
assert HOT_STEPS == HOT_SLOTS and HI_CUTS[-1] == HI and len(HI_CUTS) == COUNT_STEPS + 1
assert CHUNK_HI * CHUNKS == HI and ROWS_PER_BANK * HI <= BANK


def recommender(nc, ids, w1, b1, w2, b2, out):
    f32, f32r, bf16, i32 = mybir.dt.float32, mybir.dt.float32r, mybir.dt.bfloat16, mybir.dt.int32
    ALU, ACT = mybir.AluOpType, mybir.ActivationFunctionType

    with ExitStack() as ctx:
        def sb(name, shape, dt):
            return ctx.enter_context(nc.sbuf_tensor(name, shape, dt))

        def sem(name):
            return ctx.enter_context(nc.semaphore(name))

        ids_i = sb("ids_i", [IDS, BATCH], i32)
        lows_i = sb("lows_i", [IDS, BATCH], i32)
        wrap = lows_i[:, :].bitcast(f32)
        lows = sb("lows", [IDS, BATCH, 2], bf16)
        highs = sb("highs", [IDS, BATCH, 2], bf16)
        digit = sb("digit", [P, LO], bf16)
        hot = sb("hot", [IDS, HOT_SLOTS, HOT_ROWS, LO + HI], bf16)
        bits = sb("bits", [P, 2, HI, TILE], f32r)
        w_stage = sb("w_stage", [P, STAGES, CHUNK_HI, D], f32)
        w_parts = sb("w_parts", [P, HI, 2, D], f32r)
        w2_s = sb("w2_s", [P, D_HALVES, CLASSES], f32)
        b1_s = sb("b1_s", [P, D_HALVES], f32)
        b2_s = sb("b2_s", [P, CLASSES], f32)
        ident = sb("ident", [P, P], f32)
        h_high = sb("h_high", [TILE, D], f32)
        h = sb("h", [TILE, D], f32)
        hT = sb("hT", [P, D_HALVES, TILE], f32)
        y = sb("y", [TILE, CLASSES], f32)

        counts = ctx.enter_context(nc.psum_tensor("counts", [P, COUNT_SLOTS, 2, BANK], f32))
        acc = ctx.enter_context(nc.psum_tensor("acc", [TILE, 2, BANK], f32))
        fin = ctx.enter_context(nc.psum_tensor("fin", [P, 2 * BANK], f32))
        hT_psum = fin[:, BANK + 128:BANK + 128 + D].rearrange("p (c b) -> p c b", c=D_HALVES)

        ids_landed = sem("ids_landed")
        small_landed = sem("small_landed")
        w_landed = [sem(f"w_landed{s}") for s in range(STAGES)]
        const_made = sem("const_made")
        vec_chain = sem("vec_chain")
        digits_int = sem("digits_int")
        digits_ready = sem("digits_ready")
        w_high_ready = sem("w_high_ready")
        w_ready = sem("w_ready")
        hot_ready = sem("hot_ready")
        counted = sem("counted")
        bits_ready = sem("bits_ready")
        acc_ready = sem("acc_ready")
        h_high_ready = sem("h_high_ready")
        h_ready = sem("h_ready")
        hT_in_psum = sem("hT_in_psum")
        hT_ready = sem("hT_ready")
        fin_ready = sem("fin_ready")
        y_ready = sem("y_ready")
        y_stored = sem("y_stored")

        pieces = [(0, TILE), (TILE, BATCH)]

        def turns(eng, first, last, turn, **how):
            with eng.Fori(0, (last - first + 1) // 2) as pair:
                turn(pair * 2 + first, 1, **how)
                turn(pair * 2 + first + 1, 0, **how)

        block = ctx.enter_context(nc.Block())

        @block.sync
        def _(sp):
            sp.dma_start(ids_i[:, :], ids).then_inc(ids_landed, 16)
            for c in range(CHUNKS):
                if c >= STAGES:
                    sp.wait_ge(w_ready, c - STAGES + 1)
                sp.dma_start(w_stage[:, c % STAGES], w1[:, c * CHUNK_HI:(c + 1) * CHUNK_HI, :])\
                    .then_inc(w_landed[c % STAGES], 16)
            with sp.Fori(0, TILES) as t:
                sp.wait_ge(y_ready, t + 1)
                sp.dma_start(out[bass.ds(t * TILE, TILE), :], y[:, :]).then_inc(y_stored, 16)
            sp.wait_ge(y_stored, 16 * TILES)

        @block.gpsimd
        def _(pool):
            nc.gpsimd.iota(digit[:, :], pattern=[[1, LO]], base=0, channel_multiplier=0,
                           allow_small_or_imprecise_dtypes=True).then_inc(const_made, 1)
            nc.gpsimd.memset(ident[:, :], 0.0).then_inc(const_made, 1)
            pool.wait_ge(const_made, 2)
            nc.gpsimd.affine_select(out=ident[:, :], in_=ident[:, :], compare_op=ALU.not_equal, fill=1.0,
                                    base=0, pattern=[[-1, P]], channel_multiplier=1).then_inc(const_made, 1)

        @block.vector
        def _(dve):
            def cut(piece):
                lo, hi = pieces[piece]
                x, low = ids_i[:, lo:hi], lows_i[:, lo:hi]
                nc.vector.tensor_scalar(wrap[:, lo:hi], x, 0.0, float(N_IDS + 1), ALU.is_lt, ALU.mult)\
                    .then_inc(vec_chain, 1)
                dve.wait_ge(vec_chain, 3 * piece + 1)
                nc.vector.tensor_tensor(x, x, wrap[:, lo:hi], ALU.add).then_inc(vec_chain, 1)
                dve.wait_ge(vec_chain, 3 * piece + 2)
                nc.vector.tensor_scalar(low, x, LO - 1, None, ALU.bitwise_and).then_inc(vec_chain, 1)
                dve.wait_ge(vec_chain, 3 * piece + 3)
                nc.vector.tensor_scalar(x, x, LO_BITS, None, ALU.arith_shift_right).then_inc(digits_int, 1)

            def one_hot(t, step):
                rows = bass.ds(t * TILE + step * HOT_ROWS, HOT_ROWS)
                for digits, at, n in ((lows, 0, LO), (highs, LO, HI)):
                    last = nc.vector.tensor_tensor(
                        hot[:, step, :, at:at + n].rearrange("m b (v w) -> m b v w", w=2),
                        digits[:, rows, :].unsqueeze(2).broadcast_to([IDS, HOT_ROWS, n // 2, 2]),
                        digit[0:IDS, 0:n].rearrange("m (v w) -> m v w", w=2).unsqueeze(1)
                        .broadcast_to([IDS, HOT_ROWS, n // 2, 2]), ALU.is_equal)
                last.then_inc(hot_ready, 1)

            def one_hot_again(t, step):
                dve.wait_ge(counted, (t - 1) * COUNT_STEPS + (step + 1) * (COUNT_STEPS // HOT_STEPS))
                one_hot(t, step)

            def split_low(c):
                ks = slice(c * CHUNK_HI, (c + 1) * CHUNK_HI)
                dve.wait_ge(w_high_ready, c + 1)
                nc.vector.tensor_tensor(w_parts[:, ks, 1, :], w_stage[:, c % STAGES],
                                        w_parts[:, ks, 0, :].bitcast(f32), ALU.subtract).then_inc(w_ready, 1)

            def add_halves(t, half, first):
                dve.wait_ge(h_high_ready, t + 1)
                if not first:
                    dve.wait_ge(hT_in_psum, t)
                nc.vector.tensor_tensor(h[:, :], acc[:, half, D:2 * D], h_high[:, :], ALU.add)\
                    .then_inc(h_ready, 1)

            def finish(t, first):
                dve.wait_ge(fin_ready, t + 1)
                if not first:
                    dve.wait_ge(y_stored, t * 16)
                nc.vector.tensor_tensor(y[:, :], fin[:, 0:CLASSES], b2_s[:, :], ALU.add)\
                    .then_inc(y_ready, 1)

            def turn(t, half, hots=True, first=False):
                add_halves(t, half, first)
                for step in range(HOT_STEPS):
                    if hots:
                        one_hot_again(t + 3, step)
                    if step == 1:
                        finish(t, first)

            dve.wait_ge(ids_landed, 16)
            cut(0)
            dve.wait_ge(const_made, 1)
            dve.wait_ge(digits_ready, 1)
            one_hot(0, 0)
            one_hot(0, 1)
            cut(1)
            split_low(0)
            one_hot(0, 2)
            split_low(1)
            one_hot(0, 3)
            dve.wait_ge(digits_ready, 2)
            split_low(2)
            one_hot_again(1, 0)
            split_low(3)
            split_low(4)
            one_hot_again(1, 1)
            split_low(5)
            one_hot_again(1, 2)
            split_low(6)
            split_low(7)
            one_hot_again(1, 3)
            for step in range(HOT_STEPS):
                one_hot_again(2, step)
            dve.wait_ge(small_landed, 3 * 16)
            turn(0, 0, first=True)
            turns(dve, 1, TILES - 4, turn)
            turns(dve, TILES - 3, TILES - 2, turn, hots=False)
            turn(TILES - 1, 1, hots=False)

        @block.scalar
        def _(act):
            act.dma_start(w2_s[:, :, :], w2).then_inc(small_landed, 16)
            act.dma_start(b1_s[:, :], b1).then_inc(small_landed, 16)
            act.dma_start(b2_s[:, :], b2.broadcast_to([P, CLASSES])).then_inc(small_landed, 16)

            def widen(piece):
                lo, hi = pieces[piece]
                act.wait_ge(digits_int, piece + 1)
                for src, dst in ((lows_i, lows), (ids_i, highs)):
                    last = nc.scalar.activation(
                        dst[:, lo:hi, :], src[:, lo:hi].unsqueeze(2).broadcast_to([IDS, hi - lo, 2]), ACT.Copy)
                last.then_inc(digits_ready, 1)

            def split_high(c):
                act.wait_ge(w_landed[c % STAGES], 16 * (c // STAGES + 1))
                nc.scalar.activation(w_parts[:, c * CHUNK_HI:(c + 1) * CHUNK_HI, 0, :], w_stage[:, c % STAGES],
                                     ACT.Copy).then_inc(w_high_ready, 1)

            def to_bits(t, half, step, fresh=False):
                rows = bits[:, half, :, step * COUNT_ROWS:(step + 1) * COUNT_ROWS]
                act.wait_ge(counted, t * COUNT_STEPS + step + 1)
                if step == 0 and not fresh:
                    act.wait_ge(acc_ready, t - 1)
                nc.scalar.activation(
                    rows.rearrange("p k (x b) -> p x b k", x=2),
                    counts[:, step % COUNT_SLOTS, :, 0:ROWS_PER_BANK * HI]
                    .rearrange("p x (b k) -> p x b k", k=HI), ACT.Sign).then_inc(bits_ready, 1)

            def take_high(t, half, first):
                act.wait_ge(acc_ready, t + 1)
                if not first:
                    act.wait_ge(h_ready, t)
                nc.scalar.activation(h_high[:, :], acc[:, half, 0:D], ACT.Copy).then_inc(h_high_ready, 1)

            def take_hT(t, first):
                act.wait_ge(hT_in_psum, t + 1)
                if not first:
                    act.wait_ge(fin_ready, t)
                for c in range(D_HALVES):
                    last = nc.scalar.activation(hT[:, c, :], hT_psum[:, c, :], ACT.Identity, bias=b1_s[:, c:c + 1])
                last.then_inc(hT_ready, 1)

            def turn(t, half, bits_too=True, first=False):
                take_high(t, half, first)
                for step in range(COUNT_STEPS):
                    if bits_too:
                        to_bits(t + 2, half, step)
                    if step == 1:
                        take_hT(t, first)

            widen(0)
            to_bits(0, 0, 0, fresh=True)
            to_bits(0, 0, 1, fresh=True)
            widen(1)
            split_high(0)
            to_bits(0, 0, 2, fresh=True)
            to_bits(0, 0, 3, fresh=True)
            split_high(1)
            for step in range(4, COUNT_STEPS):
                to_bits(0, 0, step, fresh=True)
            split_high(2)
            for step in range(COUNT_STEPS):
                if step + 3 < CHUNKS:
                    split_high(step + 3)
                to_bits(1, 1, step, fresh=True)
            act.wait_ge(small_landed, 3 * 16)
            turn(0, 0, first=True)
            turns(act, 1, TILES - 4, turn)
            turn(TILES - 3, 1)
            turn(TILES - 2, 0, bits_too=False)
            turn(TILES - 1, 1, bits_too=False)

        @block.tensor
        def _(pe):
            def count(t, step, first=False):
                if step % (HOT_ROWS // COUNT_ROWS) == 0:
                    pe.wait_ge(hot_ready, t * HOT_STEPS + step // (HOT_ROWS // COUNT_ROWS) + 1)
                if not (first and step < COUNT_SLOTS):
                    pe.wait_ge(bits_ready, t * COUNT_STEPS + step - COUNT_SLOTS + 1)
                for r in range(COUNT_ROWS):
                    row = step * COUNT_ROWS + r
                    digits = hot[:, row // HOT_ROWS, row % HOT_ROWS, :]
                    at = (r % ROWS_PER_BANK) * HI
                    last = nc.tensor.matmul(counts[:, step % COUNT_SLOTS, r // ROWS_PER_BANK, at:at + HI],
                                            digits[:, 0:LO], digits[:, LO:LO + HI], start=True, stop=True)
                last.then_inc(counted, 1)

            def first_layer(t, half, step, first=False, fresh=False):
                if step == 0:
                    pe.wait_ge(bits_ready, (t + 1) * COUNT_STEPS)
                    if not fresh:
                        pe.wait_ge(h_ready, t - 1)
                for k in range(HI_CUTS[step], HI_CUTS[step + 1]):
                    if first and k % CHUNK_HI == 0:
                        pe.wait_ge(w_ready, k // CHUNK_HI + 1)
                    last = nc.tensor.matmul(acc[:, half, :], bits[:, half, k, :],
                                            w_parts[:, k].rearrange("p x d -> p (x d)"),
                                            start=(k == 0), stop=(k == HI - 1))
                if step == COUNT_STEPS - 1:
                    last.then_inc(acc_ready, 1)

            def transpose_h(t):
                pe.wait_ge(h_ready, t + 1)
                for c in range(D_HALVES):
                    last = nc.tensor.transpose(hT_psum[:, c, :], h[:, c * P:(c + 1) * P], ident[:, :])
                last.then_inc(hT_in_psum, 1)

            def second_layer(t, first=False):
                pe.wait_ge(hT_ready, t + 1)
                if not first:
                    pe.wait_ge(y_ready, t)
                for lo, hi in ((0, CUT), (CUT, CLASSES)):
                    for c in range(D_HALVES):
                        last = nc.tensor.matmul(fin[:, lo:hi], hT[:, c, :], w2_s[:, c, lo:hi],
                                                start=(c == 0), stop=(c == D_HALVES - 1))
                last.then_inc(fin_ready, 1)

            def turn(t, half, count_too=True, first=False):
                for step in range(COUNT_STEPS):
                    if count_too:
                        count(t + 2, step)
                    first_layer(t + 1, 1 - half, step, fresh=first)
                    if step == 1:
                        transpose_h(t)
                    if step == 3:
                        second_layer(t, first)

            for step in range(COUNT_STEPS):
                count(0, step, first=True)
            for step in range(COUNT_STEPS):
                count(1, step)
                first_layer(0, 0, step, first=True, fresh=True)
            pe.wait_ge(const_made, 3)
            pe.wait_ge(small_landed, 3 * 16)
            turn(0, 0, first=True)
            turns(pe, 1, TILES - 4, turn)
            turn(TILES - 3, 1)
            turn(TILES - 2, 0, count_too=False)
            transpose_h(TILES - 1)
            second_layer(TILES - 1)


def kernel(r_x, L0_rec_W1, L0_rec_b1, L0_rec_W2, L0_rec_b2):
    import numpy as np
    import concourse.bacc as bacc
    from concourse.bass_utils import run_bass_kernel_spmd

    w1 = np.zeros((HI * LO, D), np.float32)
    w1[:N_IDS] = np.asarray(L0_rec_W1).T
    arrays = {
        "ids": np.ascontiguousarray(np.asarray(r_x).T),
        "w1": np.ascontiguousarray(w1.reshape(HI, LO, D).transpose(1, 0, 2)),
        "b1": np.ascontiguousarray(np.asarray(L0_rec_b1).reshape(D_HALVES, P).T),
        "w2": np.ascontiguousarray(np.asarray(L0_rec_W2).T.reshape(D_HALVES, P, CLASSES).transpose(1, 0, 2)),
        "b2": np.ascontiguousarray(np.asarray(L0_rec_b2).reshape(1, CLASSES)),
    }
    nc = bacc.Bacc("TRN2", target_bir_lowering=False, num_devices=1)
    drams = [nc.dram_tensor(name, a.shape, mybir.dt.from_np(a.dtype), kind="ExternalInput").ap()
             for name, a in arrays.items()]
    out = nc.dram_tensor("out", (BATCH, CLASSES), mybir.dt.float32, kind="ExternalOutput").ap()
    recommender(nc, *drams, out)
    return run_bass_kernel_spmd(nc, [arrays], core_ids=[0]).results[0]["out"]
```

```python
import concourse.bass as bass
import concourse.mybir as mybir
from contextlib import ExitStack

BATCH, IDS, N_IDS, D, CLASSES = 1024, 100, 5000, 256, 625
P = 128
LO = 128
LO_BITS = 7
HI = -(-N_IDS // LO)
TILE = 128
TILES = BATCH // TILE
BANK = 512
D_HALVES = D // P
CUT = min(CLASSES, BANK)

HOT_ROWS = 32
HOT_SLOTS = 4
HOT_STEPS = TILE // HOT_ROWS
COUNT_ROWS = 16
COUNT_SLOTS = 2
COUNT_STEPS = TILE // COUNT_ROWS
ROWS_PER_BANK = COUNT_ROWS // 2
CHUNKS = 8
CHUNK_HI = HI // CHUNKS
STAGES = 3
HI_CUTS = [0, 4, 8, 13, 18, 23, 28, 34, 40]
assert HOT_STEPS == HOT_SLOTS and HI_CUTS[-1] == HI and len(HI_CUTS) == COUNT_STEPS + 1
assert CHUNK_HI * CHUNKS == HI and ROWS_PER_BANK * HI <= BANK


def recommender(nc, ids, w1, b1, w2, b2, out):
    f32, f32r, bf16, i32 = mybir.dt.float32, mybir.dt.float32r, mybir.dt.bfloat16, mybir.dt.int32
    ALU, ACT = mybir.AluOpType, mybir.ActivationFunctionType

    with ExitStack() as ctx:
        def sb(name, shape, dt):
            return ctx.enter_context(nc.sbuf_tensor(name, shape, dt))

        def sem(name):
            return ctx.enter_context(nc.semaphore(name))

        ids_i = sb("ids_i", [IDS, BATCH], i32)
        lows_i = sb("lows_i", [IDS, BATCH], i32)
        wrap = lows_i[:, :].bitcast(f32)
        lows = sb("lows", [IDS, BATCH, 2], bf16)
        highs = sb("highs", [IDS, BATCH, 2], bf16)
        digit = sb("digit", [P, LO], bf16)
        hot = sb("hot", [IDS, HOT_SLOTS, HOT_ROWS, LO + HI], bf16)
        bits = sb("bits", [P, 2, HI, TILE], f32r)
        w_stage = sb("w_stage", [P, STAGES, CHUNK_HI, D], f32)
        w_parts = sb("w_parts", [P, HI, 2, D], f32r)
        w2_s = sb("w2_s", [P, D_HALVES, CLASSES], f32)
        b1_s = sb("b1_s", [P, D_HALVES], f32)
        b2_s = sb("b2_s", [P, CLASSES], f32)
        ident = sb("ident", [P, P], f32)
        h_high = sb("h_high", [TILE, D], f32)
        h = sb("h", [TILE, D], f32)
        hT = sb("hT", [P, D_HALVES, TILE], f32)
        y = sb("y", [TILE, CLASSES], f32)

        counts = ctx.enter_context(nc.psum_tensor("counts", [P, COUNT_SLOTS, 2, BANK], f32))
        acc = ctx.enter_context(nc.psum_tensor("acc", [TILE, 2, BANK], f32))
        fin = ctx.enter_context(nc.psum_tensor("fin", [P, 2 * BANK], f32))
        hT_psum = fin[:, BANK + 128:BANK + 128 + D].rearrange("p (c b) -> p c b", c=D_HALVES)

        ids_landed = [sem(f"ids_landed{n}") for n in range(2)]
        small_landed = sem("small_landed")
        w_landed = [sem(f"w_landed{s}") for s in range(STAGES)]
        const_made = sem("const_made")
        vec_chain = sem("vec_chain")
        digits_int = sem("digits_int")
        digits_ready = sem("digits_ready")
        w_high_ready = sem("w_high_ready")
        w_ready = sem("w_ready")
        hot_ready = sem("hot_ready")
        counted = sem("counted")
        bits_ready = sem("bits_ready")
        acc_ready = sem("acc_ready")
        h_high_ready = sem("h_high_ready")
        h_ready = sem("h_ready")
        hT_in_psum = sem("hT_in_psum")
        hT_ready = sem("hT_ready")
        fin_ready = sem("fin_ready")
        y_ready = sem("y_ready")
        y_stored = sem("y_stored")

        pieces = [(0, TILE), (TILE, BATCH)]

        def turns(eng, first, last, turn, **how):
            with eng.Fori(0, (last - first + 1) // 2) as pair:
                turn(pair * 2 + first, 1, **how)
                turn(pair * 2 + first + 1, 0, **how)

        block = ctx.enter_context(nc.Block())

        @block.sync
        def _(sp):
            for n, (lo, hi) in enumerate(pieces):
                sp.dma_start(ids_i[:, lo:hi], ids[:, lo:hi]).then_inc(ids_landed[n], 16)
            for c in range(CHUNKS):
                if c >= STAGES:
                    sp.wait_ge(w_ready, c - STAGES + 1)
                sp.dma_start(w_stage[:, c % STAGES], w1[:, c * CHUNK_HI:(c + 1) * CHUNK_HI, :])\
                    .then_inc(w_landed[c % STAGES], 16)
            with sp.Fori(0, TILES) as t:
                sp.wait_ge(y_ready, t + 1)
                sp.dma_start(out[bass.ds(t * TILE, TILE), :], y[:, :]).then_inc(y_stored, 16)
            sp.wait_ge(y_stored, 16 * TILES)

        @block.gpsimd
        def _(pool):
            nc.gpsimd.iota(digit[:, :], pattern=[[1, LO]], base=0, channel_multiplier=0,
                           allow_small_or_imprecise_dtypes=True).then_inc(const_made, 1)
            nc.gpsimd.memset(ident[:, :], 0.0).then_inc(const_made, 1)
            pool.wait_ge(const_made, 2)
            nc.gpsimd.affine_select(out=ident[:, :], in_=ident[:, :], compare_op=ALU.not_equal, fill=1.0,
                                    base=0, pattern=[[-1, P]], channel_multiplier=1).then_inc(const_made, 1)

        @block.vector
        def _(dve):
            def cut(piece):
                lo, hi = pieces[piece]
                x, low = ids_i[:, lo:hi], lows_i[:, lo:hi]
                dve.wait_ge(ids_landed[piece], 16)
                nc.vector.tensor_scalar(wrap[:, lo:hi], x, 0.0, float(N_IDS + 1), ALU.is_lt, ALU.mult)\
                    .then_inc(vec_chain, 1)
                dve.wait_ge(vec_chain, 3 * piece + 1)
                nc.vector.tensor_tensor(x, x, wrap[:, lo:hi], ALU.add).then_inc(vec_chain, 1)
                dve.wait_ge(vec_chain, 3 * piece + 2)
                nc.vector.tensor_scalar(low, x, LO - 1, None, ALU.bitwise_and).then_inc(vec_chain, 1)
                dve.wait_ge(vec_chain, 3 * piece + 3)
                nc.vector.tensor_scalar(x, x, LO_BITS, None, ALU.arith_shift_right).then_inc(digits_int, 1)

            def one_hot(t, step):
                rows = bass.ds(t * TILE + step * HOT_ROWS, HOT_ROWS)
                for digits, at, n in ((lows, 0, LO), (highs, LO, HI)):
                    last = nc.vector.tensor_tensor(
                        hot[:, step, :, at:at + n].rearrange("m b (v w) -> m b v w", w=2),
                        digits[:, rows, :].unsqueeze(2).broadcast_to([IDS, HOT_ROWS, n // 2, 2]),
                        digit[0:IDS, 0:n].rearrange("m (v w) -> m v w", w=2).unsqueeze(1)
                        .broadcast_to([IDS, HOT_ROWS, n // 2, 2]), ALU.is_equal)
                last.then_inc(hot_ready, 1)

            def one_hot_again(t, step):
                dve.wait_ge(counted, (t - 1) * COUNT_STEPS + (step + 1) * (COUNT_STEPS // HOT_STEPS))
                one_hot(t, step)

            def split_low(c):
                ks = slice(c * CHUNK_HI, (c + 1) * CHUNK_HI)
                dve.wait_ge(w_high_ready, c + 1)
                nc.vector.tensor_tensor(w_parts[:, ks, 1, :], w_stage[:, c % STAGES],
                                        w_parts[:, ks, 0, :].bitcast(f32), ALU.subtract).then_inc(w_ready, 1)

            def add_halves(t, half, first):
                dve.wait_ge(h_high_ready, t + 1)
                if not first:
                    dve.wait_ge(hT_in_psum, t)
                nc.vector.tensor_tensor(h[:, :], acc[:, half, D:2 * D], h_high[:, :], ALU.add)\
                    .then_inc(h_ready, 1)

            def finish(t, first):
                dve.wait_ge(fin_ready, t + 1)
                if not first:
                    dve.wait_ge(y_stored, t * 16)
                nc.vector.tensor_tensor(y[:, :], fin[:, 0:CLASSES], b2_s[:, :], ALU.add)\
                    .then_inc(y_ready, 1)

            def turn(t, half, hots=True, first=False):
                for step in range(HOT_STEPS):
                    if hots:
                        one_hot_again(t + 2, step)
                    if step == 1:
                        add_halves(t, half, first)
                finish(t, first)

            cut(0)
            dve.wait_ge(const_made, 1)
            dve.wait_ge(digits_ready, 1)
            for step in range(HOT_STEPS - 1):
                one_hot(0, step)
            cut(1)
            one_hot(0, HOT_STEPS - 1)
            dve.wait_ge(digits_ready, 2)
            for step in range(HOT_STEPS):
                split_low(2 * step)
                split_low(2 * step + 1)
                one_hot_again(1, step)
            dve.wait_ge(digits_ready, TILES)
            dve.wait_ge(small_landed, 3 * 16)
            turn(0, 0, first=True)
            turns(dve, 1, TILES - 4, turn)
            turn(TILES - 3, 1)
            turn(TILES - 2, 0, hots=False)
            turn(TILES - 1, 1, hots=False)

        @block.scalar
        def _(act):
            act.dma_start(w2_s[:, :, :], w2).then_inc(small_landed, 16)
            act.dma_start(b1_s[:, :], b1).then_inc(small_landed, 16)
            act.dma_start(b2_s[:, :], b2.broadcast_to([P, CLASSES])).then_inc(small_landed, 16)

            def widen(t):
                lo, hi = t * TILE, (t + 1) * TILE
                act.wait_ge(digits_int, 1 if hi <= pieces[0][1] else 2)
                for src, dst in ((lows_i, lows), (ids_i, highs)):
                    last = nc.scalar.activation(
                        dst[:, lo:hi, :], src[:, lo:hi].unsqueeze(2).broadcast_to([IDS, hi - lo, 2]), ACT.Copy)
                last.then_inc(digits_ready, 1)

            def split_high(c):
                act.wait_ge(w_landed[c % STAGES], 16 * (c // STAGES + 1))
                nc.scalar.activation(w_parts[:, c * CHUNK_HI:(c + 1) * CHUNK_HI, 0, :], w_stage[:, c % STAGES],
                                     ACT.Copy).then_inc(w_high_ready, 1)

            def to_bits(t, half, step, fresh=False):
                rows = bits[:, half, :, step * COUNT_ROWS:(step + 1) * COUNT_ROWS]
                act.wait_ge(counted, t * COUNT_STEPS + step + 1)
                if step == 0 and not fresh:
                    act.wait_ge(acc_ready, t - 1)
                nc.scalar.activation(
                    rows.rearrange("p k (x b) -> p x b k", x=2),
                    counts[:, step % COUNT_SLOTS, :, 0:ROWS_PER_BANK * HI]
                    .rearrange("p x (b k) -> p x b k", k=HI), ACT.Sign).then_inc(bits_ready, 1)

            def take_high(t, half, first):
                act.wait_ge(acc_ready, t + 1)
                if not first:
                    act.wait_ge(h_ready, t)
                nc.scalar.activation(h_high[:, :], acc[:, half, 0:D], ACT.Copy).then_inc(h_high_ready, 1)

            def take_hT(t, first):
                act.wait_ge(hT_in_psum, t + 1)
                if not first:
                    act.wait_ge(fin_ready, t)
                for c in range(D_HALVES):
                    last = nc.scalar.activation(hT[:, c, :], hT_psum[:, c, :], ACT.Identity, bias=b1_s[:, c:c + 1])
                last.then_inc(hT_ready, 1)

            def turn(t, half, bits_too=True, first=False):
                take_high(t, half, first)
                for step in range(COUNT_STEPS):
                    if bits_too:
                        to_bits(t + 2, half, step)
                    if step == 1:
                        take_hT(t, first)

            widen(0)
            for step in range(COUNT_STEPS):
                if step % 2 == 0 and step // 2 < STAGES:
                    split_high(step // 2)
                if step == COUNT_STEPS - 4:
                    widen(1)
                to_bits(0, 0, step, fresh=True)
            split_high(3)
            for step in range(COUNT_STEPS):
                if step < CHUNKS - 4:
                    split_high(step + 4)
                to_bits(1, 1, step, fresh=True)
                if step + 2 < TILES:
                    widen(step + 2)
            act.wait_ge(small_landed, 3 * 16)
            turn(0, 0, first=True)
            turns(act, 1, TILES - 4, turn)
            turn(TILES - 3, 1)
            turn(TILES - 2, 0, bits_too=False)
            turn(TILES - 1, 1, bits_too=False)

        @block.tensor
        def _(pe):
            def count(t, step, first=False):
                if step % (HOT_ROWS // COUNT_ROWS) == 0:
                    pe.wait_ge(hot_ready, t * HOT_STEPS + step // (HOT_ROWS // COUNT_ROWS) + 1)
                if not (first and step < COUNT_SLOTS):
                    pe.wait_ge(bits_ready, t * COUNT_STEPS + step - COUNT_SLOTS + 1)
                for r in range(COUNT_ROWS):
                    row = step * COUNT_ROWS + r
                    digits = hot[:, row // HOT_ROWS, row % HOT_ROWS, :]
                    at = (r % ROWS_PER_BANK) * HI
                    last = nc.tensor.matmul(counts[:, step % COUNT_SLOTS, r // ROWS_PER_BANK, at:at + HI],
                                            digits[:, 0:LO], digits[:, LO:LO + HI], start=True, stop=True)
                last.then_inc(counted, 1)

            def first_layer(t, half, step, first=False, fresh=False):
                if step == 0:
                    pe.wait_ge(bits_ready, (t + 1) * COUNT_STEPS)
                    if not fresh:
                        pe.wait_ge(h_ready, t - 1)
                for k in range(HI_CUTS[step], HI_CUTS[step + 1]):
                    if first and k % CHUNK_HI == 0:
                        pe.wait_ge(w_ready, k // CHUNK_HI + 1)
                    last = nc.tensor.matmul(acc[:, half, :], bits[:, half, k, :],
                                            w_parts[:, k].rearrange("p x d -> p (x d)"),
                                            start=(k == 0), stop=(k == HI - 1))
                if step == COUNT_STEPS - 1:
                    last.then_inc(acc_ready, 1)

            def transpose_h(t):
                pe.wait_ge(h_ready, t + 1)
                for c in range(D_HALVES):
                    last = nc.tensor.transpose(hT_psum[:, c, :], h[:, c * P:(c + 1) * P], ident[:, :])
                last.then_inc(hT_in_psum, 1)

            def second_layer(t, first=False):
                pe.wait_ge(hT_ready, t + 1)
                if not first:
                    pe.wait_ge(y_ready, t)
                for lo, hi in ((0, CUT), (CUT, CLASSES)):
                    for c in range(D_HALVES):
                        last = nc.tensor.matmul(fin[:, lo:hi], hT[:, c, :], w2_s[:, c, lo:hi],
                                                start=(c == 0), stop=(c == D_HALVES - 1))
                last.then_inc(fin_ready, 1)

            def turn(t, half, count_too=True, first=False):
                for step in range(COUNT_STEPS):
                    if count_too:
                        count(t + 2, step)
                    first_layer(t + 1, 1 - half, step, fresh=first)
                    if step == 1:
                        transpose_h(t)
                    if step == 3:
                        second_layer(t, first)

            for step in range(COUNT_STEPS):
                count(0, step, first=True)
            for step in range(COUNT_STEPS):
                first_layer(0, 0, step, first=True, fresh=True)
                if step % 2 == 1:
                    count(1, step - 1)
                    count(1, step)
            pe.wait_ge(const_made, 3)
            pe.wait_ge(small_landed, 3 * 16)
            turn(0, 0, first=True)
            turns(pe, 1, TILES - 4, turn)
            turn(TILES - 3, 1)
            turn(TILES - 2, 0, count_too=False)
            transpose_h(TILES - 1)
            second_layer(TILES - 1)


def kernel(r_x, L0_rec_W1, L0_rec_b1, L0_rec_W2, L0_rec_b2):
    import numpy as np
    import concourse.bacc as bacc
    from concourse.bass_utils import run_bass_kernel_spmd

    w1 = np.zeros((HI * LO, D), np.float32)
    w1[:N_IDS] = np.asarray(L0_rec_W1).T
    arrays = {
        "ids": np.ascontiguousarray(np.asarray(r_x).T),
        "w1": np.ascontiguousarray(w1.reshape(HI, LO, D).transpose(1, 0, 2)),
        "b1": np.ascontiguousarray(np.asarray(L0_rec_b1).reshape(D_HALVES, P).T),
        "w2": np.ascontiguousarray(np.asarray(L0_rec_W2).T.reshape(D_HALVES, P, CLASSES).transpose(1, 0, 2)),
        "b2": np.ascontiguousarray(np.asarray(L0_rec_b2).reshape(1, CLASSES)),
    }
    nc = bacc.Bacc("TRN2", target_bir_lowering=False, num_devices=1)
    drams = [nc.dram_tensor(name, a.shape, mybir.dt.from_np(a.dtype), kind="ExternalInput").ap()
             for name, a in arrays.items()]
    out = nc.dram_tensor("out", (BATCH, CLASSES), mybir.dt.float32, kind="ExternalOutput").ap()
    recommender(nc, *drams, out)
    return run_bass_kernel_spmd(nc, [arrays], core_ids=[0]).results[0]["out"]
```

```python
import concourse.bass as bass
import concourse.mybir as mybir
from contextlib import ExitStack

BATCH, IDS, N_IDS, D, CLASSES = 1024, 100, 5000, 256, 625
P = 128
LO = 128
LO_BITS = 7
HI = -(-N_IDS // LO)
TILE = 128
TILES = BATCH // TILE
BANK = 512
D_HALVES = D // P
CUT = min(CLASSES, BANK)
BANKS_OF_CLASSES = ((0, CUT), (CUT, CLASSES))

HOT_ROWS = 32
HOT_SLOTS = 4
HOT_STEPS = TILE // HOT_ROWS
COUNT_ROWS = 16
COUNT_SLOTS = 2
COUNT_STEPS = TILE // COUNT_ROWS
ROWS_PER_BANK = COUNT_ROWS // 2
CHUNKS = 10
CHUNK_HI = HI // CHUNKS
PE_CHUNKS = [0, 1, 2]
DVE_CHUNKS = [c for c in range(CHUNKS) if c not in PE_CHUNKS]
DVE_SPLITS = [[3, 4, 5], [6, 7], [8, 9], []]
FIRST_TILE = [[0, 1], [6, 7], [8], [9], [2, 3, 4, 5]]
WHOLE_CHUNKS = [6, 7, 8, 9]
WARM_UP = 12
HI_BEFORE = [11, 20, 28, 34]
assert HOT_STEPS == HOT_SLOTS and 2 * len(HI_BEFORE) == COUNT_STEPS
assert sum(DVE_SPLITS, []) == DVE_CHUNKS and sorted(sum(FIRST_TILE, [])) == list(range(CHUNKS))
assert TILES % 2 == 0 and CHUNK_HI * CHUNKS == HI and CHUNK_HI * D == 2 * BANK and ROWS_PER_BANK * HI <= BANK


def recommender(nc, ids, w1, b1, w2, b2, out):
    f32, f32r, bf16, i32 = mybir.dt.float32, mybir.dt.float32r, mybir.dt.bfloat16, mybir.dt.int32
    ALU, ACT = mybir.AluOpType, mybir.ActivationFunctionType

    with ExitStack() as ctx:
        def sb(name, shape, dt):
            return ctx.enter_context(nc.sbuf_tensor(name, shape, dt))

        def sem(name):
            return ctx.enter_context(nc.semaphore(name))

        ids_i = sb("ids_i", [IDS, BATCH], i32)
        lows_i = sb("lows_i", [IDS, BATCH], i32)
        wrap = lows_i[:, :].bitcast(f32)
        lows = sb("lows", [IDS, BATCH, 2], bf16)
        highs = sb("highs", [IDS, BATCH, 2], bf16)
        digit = sb("digit", [P, LO], bf16)
        hot = sb("hot", [IDS, HOT_SLOTS, HOT_ROWS, LO + HI], bf16)
        bits = sb("bits", [P, 2, HI, TILE], f32r)
        with nc.sbuf_tensor("w1_place", [P, HI, 2, D], f32) as w1_place:
            w1_s = w1_place[:, :, 1, :]
        w_parts = sb("w_parts", [P, HI, 2, D], f32r)
        w2_s = sb("w2_s", [P, D_HALVES, CLASSES], f32)
        b1_s = sb("b1_s", [P, D_HALVES], f32)
        b2_s = sb("b2_s", [P, CLASSES], f32)
        ident = sb("ident", [P, P], f32)
        neg_ident = sb("neg_ident", [P, P], f32r)
        h_high = sb("h_high", [TILE, D], f32)
        h = sb("h", [TILE, D], f32)
        hT = sb("hT", [P, 2, D_HALVES, TILE], f32)
        y = sb("y", [TILE, 2, CLASSES], f32)

        counts = ctx.enter_context(nc.psum_tensor("counts", [P, COUNT_SLOTS, 2, BANK], f32))
        acc = ctx.enter_context(nc.psum_tensor("acc", [TILE, 2 * BANK], f32))
        fin = ctx.enter_context(nc.psum_tensor("fin", [P, 2 * BANK], f32))

        fin_last = counts[:, 0].rearrange("p x n -> p (x n)")

        def diff(c):
            return (fin, acc)[PE_CHUNKS.index(c) % 2]

        hT_psum = [acc[:, half * BANK:half * BANK + D].rearrange("p (c b) -> p c b", c=D_HALVES)
                   for half in range(2)]

        ids_landed = [sem(f"ids_landed{n}") for n in range(3)]
        small_landed = sem("small_landed")
        w_landed = [sem(f"w_landed{c}") for c in range(CHUNKS)]
        const_made = sem("const_made")
        vec_chain = sem("vec_chain")
        digits_int = sem("digits_int")
        first_digits_ready = sem("first_digits_ready")
        digits_ready = sem("digits_ready")
        w_high_ready = sem("w_high_ready")
        neg_ident_ready = sem("neg_ident_ready")
        w_diff = sem("w_diff")
        w_low_pe = sem("w_low_pe")
        w_low_dve = sem("w_low_dve")
        w1_used = sem("w1_used")
        hot_ready = sem("hot_ready")
        counted = sem("counted")
        bits_ready = sem("bits_ready")
        acc_ready = sem("acc_ready")
        h_high_ready = sem("h_high_ready")
        h_ready = sem("h_ready")
        hT_in_psum = sem("hT_in_psum")
        hT_ready = sem("hT_ready")
        fin_ready = sem("fin_ready")
        y_ready = sem("y_ready")
        y_stored = [sem(f"y_stored{half}") for half in range(2)]

        pieces = [(0, TILE), (TILE, 2 * TILE), (2 * TILE, BATCH)]

        def turns(eng, first, last, turn, **how):
            with eng.Fori(0, (last - first + 1) // 2) as pair:
                turn(pair * 2 + first, 1, **how)
                turn(pair * 2 + first + 1, 0, **how)

        def widen(copy, t):
            rows = bass.ds(t * TILE, TILE)
            for ints, to in ((lows_i, lows), (ids_i, highs)):
                last = copy(to[:, rows, :], ints[:, rows].unsqueeze(2).broadcast_to([IDS, TILE, 2]))
            return last

        block = ctx.enter_context(nc.Block())

        @block.sync
        def _(sp):
            for c in range(CHUNKS):
                if c < len(pieces):
                    lo, hi = pieces[c]
                    sp.dma_start(ids_i[:, lo:hi], ids[:, lo:hi]).then_inc(ids_landed[c], 16)
                ks = slice(c * CHUNK_HI, (c + 1) * CHUNK_HI)
                sp.dma_start(w1_s[:, ks, :], w1[:, ks, :]).then_inc(w_landed[c], 16)

            def store(t, half, lo=0, hi=CLASSES):
                sp.dma_start(out[bass.ds(t * TILE, TILE), lo:hi], y[:, half, lo:hi]).then_inc(y_stored[half], 16)

            with sp.Fori(0, TILES // 2 - 1) as pair:
                for half in range(2):
                    sp.wait_ge(y_ready, pair * 2 + half + 1)
                    store(pair * 2 + half, half)
            sp.wait_ge(y_ready, TILES - 1)
            store(TILES - 2, 0)
            sp.wait_ge(y_ready, TILES)
            store(TILES - 1, 1, 0, CUT)
            sp.wait_ge(y_ready, TILES + 1)
            store(TILES - 1, 1, CUT, CLASSES)
            sp.wait_ge(y_stored[0], 16 * (TILES // 2))
            sp.wait_ge(y_stored[1], 16 * (TILES // 2 + 1))

        @block.gpsimd
        def _(pool):
            nc.gpsimd.iota(digit[:, :], pattern=[[1, LO]], base=0, channel_multiplier=0,
                           allow_small_or_imprecise_dtypes=True).then_inc(const_made, 1)
            nc.gpsimd.memset(ident[:, :], 0.0).then_inc(const_made, 1)
            pool.wait_ge(const_made, 2)
            nc.gpsimd.affine_select(out=ident[:, :], in_=ident[:, :], compare_op=ALU.not_equal, fill=1.0,
                                    base=0, pattern=[[-1, P]], channel_multiplier=1).then_inc(const_made, 1)

        @block.vector
        def _(dve):
            def cut(t, part):
                rows = bass.ds(t * TILE, TILE)
                x, low = ids_i[:, rows], lows_i[:, rows]
                if part == 0:
                    nc.vector.tensor_scalar(wrap[:, rows], x, 0.0, float(N_IDS + 1), ALU.is_lt, ALU.mult)\
                        .then_inc(vec_chain, 1)
                elif part == 1:
                    dve.wait_ge(vec_chain, 3 * t + 1)
                    nc.vector.tensor_tensor(x, x, wrap[:, rows], ALU.add).then_inc(vec_chain, 1)
                elif part == 2:
                    dve.wait_ge(vec_chain, 3 * t + 2)
                    nc.vector.tensor_scalar(low, x, LO - 1, None, ALU.bitwise_and).then_inc(vec_chain, 1)
                else:
                    dve.wait_ge(vec_chain, 3 * t + 3)
                    nc.vector.tensor_scalar(x, x, LO_BITS, None, ALU.arith_shift_right).then_inc(digits_int, 1)

            def one_hot(t, step):
                rows = bass.ds(t * TILE + step * HOT_ROWS, HOT_ROWS)
                for digits, at, n in ((lows, 0, LO), (highs, LO, HI)):
                    last = nc.vector.tensor_tensor(
                        hot[:, step, :, at:at + n].rearrange("m b (v w) -> m b v w", w=2),
                        digits[:, rows, :].unsqueeze(2).broadcast_to([IDS, HOT_ROWS, n // 2, 2]),
                        digit[0:IDS, 0:n].rearrange("m (v w) -> m v w", w=2).unsqueeze(1)
                        .broadcast_to([IDS, HOT_ROWS, n // 2, 2]), ALU.is_equal)
                last.then_inc(hot_ready, 1)

            def one_hot_again(t, step):
                dve.wait_ge(counted, (t - 1) * COUNT_STEPS + (step + 1) * (COUNT_STEPS // HOT_STEPS))
                if step == 0:
                    dve.wait_ge(digits_ready, t)
                one_hot(t, step)

            def split_low(c):
                ks = slice(c * CHUNK_HI, (c + 1) * CHUNK_HI)
                dve.wait_ge(w_high_ready, c + 1)
                if c in WHOLE_CHUNKS:
                    dve.wait_ge(w1_used, WHOLE_CHUNKS.index(c) + 1)
                nc.vector.tensor_tensor(w_parts[:, ks, 1, :], w1_s[:, ks, :],
                                        w_parts[:, ks, 0, :].bitcast(f32), ALU.subtract)\
                    .then_inc(w_low_dve, 1)

            def add_halves(t, half, first=False):
                dve.wait_ge(h_high_ready, t + 1)
                if not first:
                    dve.wait_ge(hT_in_psum, t)
                nc.vector.tensor_tensor(h[:, :], acc[:, half * BANK + D:half * BANK + 2 * D], h_high[:, :], ALU.add)\
                    .then_inc(h_ready, 1)

            def finish(t, half, fresh=False):
                dve.wait_ge(fin_ready, t + 1)
                if not fresh:
                    dve.wait_ge(y_stored[half], (t - half) * 8)
                nc.vector.tensor_tensor(y[:, half, :], fin[:, 0:CLASSES], b2_s[:, :], ALU.add)\
                    .then_inc(y_ready, 1)

            def turn(t, half, cuts=True, first=False, fresh=False):
                for step in range(HOT_STEPS):
                    for c in DVE_SPLITS[step] if first else []:
                        split_low(c)
                    if cuts:
                        if step < 3:
                            cut(t + 3, step)
                        if step == 2:
                            cut(t + 3, 3)
                    one_hot_again(t + 2, step)
                    if step == 1:
                        add_halves(t, half, first)
                finish(t, half, fresh or first)

            dve.wait_ge(ids_landed[0], 16)
            for part in range(4):
                cut(0, part)
            dve.wait_ge(const_made, 1)
            dve.wait_ge(digits_int, 1)
            widen(nc.vector.tensor_copy, 0).then_inc(first_digits_ready, 1)
            dve.wait_ge(first_digits_ready, 1)
            one_hot(0, 0)
            dve.wait_ge(ids_landed[1], 16)
            cut(1, 0)
            one_hot(0, 1)
            cut(1, 1)
            one_hot(0, 2)
            cut(1, 2)
            cut(1, 3)
            one_hot(0, 3)
            dve.wait_ge(ids_landed[2], 16)
            for step in range(HOT_STEPS):
                one_hot_again(1, step)
                if step < 3:
                    cut(2, step)
                if step == 2:
                    cut(2, 3)
            dve.wait_ge(small_landed, 3 * 16)
            turn(0, 0, first=True)
            turn(1, 1, fresh=True)
            turn(2, 0)
            turns(dve, 3, TILES - 4, turn)
            turn(TILES - 3, 1, cuts=False)
            add_halves(TILES - 2, 0)
            add_halves(TILES - 1, 1)
            finish(TILES - 2, 0)
            for part, (lo, hi) in enumerate(BANKS_OF_CLASSES):
                if part == 0:
                    dve.wait_ge(y_stored[1], (TILES // 2 - 1) * 16)
                dve.wait_ge(fin_ready, TILES + part)
                nc.vector.tensor_tensor(y[:, 1, lo:hi], fin_last[:, lo:hi], b2_s[:, lo:hi], ALU.add)\
                    .then_inc(y_ready, 1)

        @block.scalar
        def _(act):
            act.dma_start(w2_s[:, :, :], w2).then_inc(small_landed, 16)
            act.dma_start(b1_s[:, :], b1).then_inc(small_landed, 16)
            act.dma_start(b2_s[:, :], b2.broadcast_to([P, CLASSES])).then_inc(small_landed, 16)

            def widen_tile(t):
                act.wait_ge(digits_int, t + 1)
                widen(lambda to, ints: nc.scalar.activation(to, ints, ACT.Copy), t).then_inc(digits_ready, 1)

            def split_high(c):
                ks = slice(c * CHUNK_HI, (c + 1) * CHUNK_HI)
                act.wait_ge(w_landed[c], 16)
                nc.scalar.activation(w_parts[:, ks, 0, :], w1_s[:, ks, :], ACT.Copy).then_inc(w_high_ready, 1)

            def take_low(c):
                act.wait_ge(w_diff, PE_CHUNKS.index(c) + 1)
                nc.scalar.activation(w_parts[:, c * CHUNK_HI:(c + 1) * CHUNK_HI, 1, :],
                                     diff(c)[:, :].rearrange("p (k d) -> p k d", d=D), ACT.Copy)\
                    .then_inc(w_low_pe, 1)

            def to_bits(t, half, step, fresh=False):
                rows = bits[:, half, :, step * COUNT_ROWS:(step + 1) * COUNT_ROWS]
                act.wait_ge(counted, t * COUNT_STEPS + step + 1)
                if step == 0 and not fresh:
                    act.wait_ge(acc_ready, t - 1)
                nc.scalar.activation(
                    rows.rearrange("p k (x b) -> p x b k", x=2),
                    counts[:, step % COUNT_SLOTS, :, 0:ROWS_PER_BANK * HI]
                    .rearrange("p x (b k) -> p x b k", k=HI), ACT.Sign).then_inc(bits_ready, 1)

            def take_high(t, half, first):
                act.wait_ge(acc_ready, t + 1)
                if not first:
                    act.wait_ge(h_ready, t)
                nc.scalar.activation(h_high[:, :], acc[:, half * BANK:half * BANK + D], ACT.Copy)\
                    .then_inc(h_high_ready, 1)

            def take_hT(t, half):
                act.wait_ge(hT_in_psum, t + 1)
                for c in range(D_HALVES):
                    last = nc.scalar.activation(hT[:, half, c, :], hT_psum[half][:, c, :], ACT.Identity,
                                                bias=b1_s[:, c:c + 1])
                last.then_inc(hT_ready, 1)

            def turn(t, half, bits_too=True, widen_too=True, first=False):
                take_high(t, half, first)
                for step in range(COUNT_STEPS):
                    if bits_too:
                        to_bits(t + 2, half, step)
                    if step == 3:
                        take_hT(t, half)
                    if bits_too and widen_too and step == 3:
                        widen_tile(t + 3)

            act.wait_ge(const_made, 3)
            nc.scalar.activation(neg_ident[:, :], ident[:, :], ACT.Copy, scale=-1.0).then_inc(neg_ident_ready, 1)
            split_high(0)
            split_high(1)
            to_bits(0, 0, 0, fresh=True)
            take_low(0)
            to_bits(0, 0, 1, fresh=True)
            split_high(2)
            to_bits(0, 0, 2, fresh=True)
            widen_tile(1)
            to_bits(0, 0, 3, fresh=True)
            take_low(1)
            for step in range(4, COUNT_STEPS):
                to_bits(0, 0, step, fresh=True)
            take_low(2)
            for step in range(COUNT_STEPS):
                if step == 3:
                    widen_tile(2)
                to_bits(1, 1, step, fresh=True)
                if step < 7:
                    split_high(step + 3)
            act.wait_ge(small_landed, 3 * 16)
            turn(0, 0, first=True)
            turns(act, 1, TILES - 4, turn)
            turn(TILES - 3, 1, widen_too=False)
            turn(TILES - 2, 0, bits_too=False)
            turn(TILES - 1, 1, bits_too=False)

        @block.tensor
        def _(pe):
            def count(t, step, first=False):
                if step % (HOT_ROWS // COUNT_ROWS) == 0:
                    pe.wait_ge(hot_ready, t * HOT_STEPS + step // (HOT_ROWS // COUNT_ROWS) + 1)
                if not (first and step < COUNT_SLOTS):
                    pe.wait_ge(bits_ready, t * COUNT_STEPS + step - COUNT_SLOTS + 1)
                for r in range(COUNT_ROWS):
                    row = step * COUNT_ROWS + r
                    digits = hot[:, row // HOT_ROWS, row % HOT_ROWS, :]
                    at = (r % ROWS_PER_BANK) * HI
                    last = nc.tensor.matmul(counts[:, step % COUNT_SLOTS, r // ROWS_PER_BANK, at:at + HI],
                                            digits[:, 0:LO], digits[:, LO:LO + HI], start=True, stop=True)
                last.then_inc(counted, 1)

            def await_low(c):
                if c in PE_CHUNKS:
                    pe.wait_ge(w_low_pe, PE_CHUNKS.index(c) + 1)
                else:
                    pe.wait_ge(w_low_dve, DVE_CHUNKS.index(c) + 1)

            def first_layer_begins(t, fresh=False):
                pe.wait_ge(bits_ready, (t + 1) * COUNT_STEPS)
                if not fresh:
                    pe.wait_ge(h_ready, t - 1)

            def first_layer(t, half, lo, hi, split=True):
                for k in range(lo, hi):
                    if not split and k % CHUNK_HI == 0:
                        await_low(k // CHUNK_HI)
                    last = nc.tensor.matmul(acc[:, half * BANK:(half + 1) * BANK], bits[:, half, k, :],
                                            w_parts[:, k].rearrange("p x d -> p (x d)"),
                                            start=(k == 0), stop=(k == HI - 1))
                if hi == HI:
                    last.then_inc(acc_ready, 1)

            def first_layer_of_first_tile(c):
                for k in range(c * CHUNK_HI, (c + 1) * CHUNK_HI):
                    ends = c == FIRST_TILE[-1][-1] and (k + 1) % CHUNK_HI == 0
                    if c in WHOLE_CHUNKS:
                        if k % CHUNK_HI == 0:
                            pe.wait_ge(w_landed[c], 16)
                        last = nc.tensor.matmul(acc[:, 0:D], bits[:, 0, k, :].bitcast(f32), w1_s[:, k, :],
                                                start=False, stop=False)
                    else:
                        if k % CHUNK_HI == 0:
                            await_low(c)
                        last = nc.tensor.matmul(acc[:, 0:BANK], bits[:, 0, k, :],
                                                w_parts[:, k].rearrange("p x d -> p (x d)"),
                                                start=(k == 0), stop=ends)
                if c in WHOLE_CHUNKS:
                    last.then_inc(w1_used, 1)
                elif ends:
                    last.then_inc(acc_ready, 1)

            def transpose_h(t, half):
                pe.wait_ge(h_ready, t + 1)
                for c in range(D_HALVES):
                    last = nc.tensor.transpose(hT_psum[half][:, c, :], h[:, c * P:(c + 1) * P], ident[:, :])
                last.then_inc(hT_in_psum, 1)

            def products(to, half, part, c):
                lo, hi = BANKS_OF_CLASSES[part]
                return nc.tensor.matmul(to[:, lo:hi], hT[:, half, c, :], w2_s[:, c, lo:hi],
                                        start=(c == 0), stop=(c == D_HALVES - 1))

            def second_layer(t, half, first=False):
                pe.wait_ge(hT_ready, t + 1)
                if not first:
                    pe.wait_ge(y_ready, t)
                for part in range(2):
                    for c in range(D_HALVES):
                        last = products(fin, half, part, c)
                last.then_inc(fin_ready, 1)

            def turn(t, half, count_too=True, first=False):
                done = 0
                first_layer_begins(t + 1, fresh=first)
                for n, before in enumerate(HI_BEFORE):
                    first_layer(t + 1, 1 - half, done, before, split=not first)
                    done = before
                    if n == 2 and count_too:
                        second_layer(t, half, first)
                    if count_too:
                        count(t + 2, 2 * n)
                        count(t + 2, 2 * n + 1)
                    if n == 1:
                        transpose_h(t, half)
                first_layer(t + 1, 1 - half, done, HI, split=not first)

            def subtract_high(c):
                pe.wait_ge(w_high_ready, c + 1)
                n = PE_CHUNKS.index(c)
                if n >= 2:
                    pe.wait_ge(w_low_pe, n - 1)
                k0, per_bank = c * CHUNK_HI, CHUNK_HI // 2
                for bank in range(2):
                    ks = slice(k0 + bank * per_bank, k0 + (bank + 1) * per_bank)
                    to = diff(c)[:, bank * BANK:(bank + 1) * BANK]
                    nc.tensor.matmul(to, ident[:, :], w1_s[:, ks, :], start=True, stop=False)
                    last = nc.tensor.matmul(to, neg_ident[:, :], w_parts[:, ks, 0, :], start=False, stop=True)
                last.then_inc(w_diff, 1)

            pe.wait_ge(const_made, 3)
            for _ in range(WARM_UP):
                nc.tensor.matmul(fin[:, 0:P], ident[:, :], ident[:, :], start=True, stop=True)
            pe.wait_ge(neg_ident_ready, 1)
            for n in range(COUNT_STEPS // 2):
                if n < len(PE_CHUNKS):
                    subtract_high(PE_CHUNKS[n])
                count(0, 2 * n, first=True)
                count(0, 2 * n + 1, first=True)
            first_layer_begins(0, fresh=True)
            pe.wait_ge(w_low_pe, 2)
            for n, chunks in enumerate(FIRST_TILE):
                for c in chunks:
                    first_layer_of_first_tile(c)
                if n < COUNT_STEPS // 2:
                    count(1, 2 * n)
                    count(1, 2 * n + 1)
            pe.wait_ge(small_landed, 3 * 16)
            turn(0, 0, first=True)
            turns(pe, 1, TILES - 4, turn)
            turn(TILES - 3, 1)
            turn(TILES - 2, 0, count_too=False)
            pe.wait_ge(hT_ready, TILES - 1)
            pe.wait_ge(y_ready, TILES - 2)
            products(fin, 0, 1, 0)
            products(fin, 0, 1, 1)
            products(fin, 0, 0, 0)
            transpose_h(TILES - 1, 1)
            products(fin, 0, 0, 1).then_inc(fin_ready, 1)
            pe.wait_ge(hT_ready, TILES)
            for part in range(2):
                products(fin_last, 1, part, 0)
                products(fin_last, 1, part, 1).then_inc(fin_ready, 1)


def kernel(r_x, L0_rec_W1, L0_rec_b1, L0_rec_W2, L0_rec_b2):
    import numpy as np
    import concourse.bacc as bacc
    from concourse.bass_utils import run_bass_kernel_spmd

    w1 = np.zeros((HI * LO, D), np.float32)
    w1[:N_IDS] = np.asarray(L0_rec_W1).T
    arrays = {
        "ids": np.ascontiguousarray(np.asarray(r_x).T),
        "w1": np.ascontiguousarray(w1.reshape(HI, LO, D).transpose(1, 0, 2)),
        "b1": np.ascontiguousarray(np.asarray(L0_rec_b1).reshape(D_HALVES, P).T),
        "w2": np.ascontiguousarray(np.asarray(L0_rec_W2).T.reshape(D_HALVES, P, CLASSES).transpose(1, 0, 2)),
        "b2": np.ascontiguousarray(np.asarray(L0_rec_b2).reshape(1, CLASSES)),
    }
    nc = bacc.Bacc("TRN2", target_bir_lowering=False, num_devices=1)
    drams = [nc.dram_tensor(name, a.shape, mybir.dt.from_np(a.dtype), kind="ExternalInput").ap()
             for name, a in arrays.items()]
    out = nc.dram_tensor("out", (BATCH, CLASSES), mybir.dt.float32, kind="ExternalOutput").ap()
    recommender(nc, *drams, out)
    return run_bass_kernel_spmd(nc, [arrays], core_ids=[0]).results[0]["out"]
```
